# Optimizing a Trainium2 kernel written in Bass

```python
import numpy as np
import jax
import jax.numpy as jnp

def _softmax(x, axis=-1):
    return jax.nn.softmax(x, axis=axis)

def _gelu(x):
    return jax.nn.gelu(x, approximate=True)

def _silu(x):
    return jax.nn.silu(x)

def _sigmoid(x):
    return jax.nn.sigmoid(x)

def _layernorm(x, axis=-1, eps=1e-05):
    m = jnp.mean(x, axis=axis, keepdims=True)
    v = jnp.var(x, axis=axis, keepdims=True)
    return (x - m) / jnp.sqrt(v + eps)

def _scatter_add(tgt, idx, src, axis=0):
    return tgt.at[idx].add(src)

def _segment_sum(src, seg, n):
    return jax.ops.segment_sum(src, seg, n)
kernel_name = 'mk_xattn_seq_d2_seqx_r8_f1928b'

def setup_inputs(seed: int=0):
    np.random.seed(seed)
    _w = jnp.asarray

    def _rec_inputs():
        import jax
        import jax.numpy as jnp
        _rk = jax.random.key(seed)
        x = 0.0002279 + 0.9999 * jax.random.normal(jax.random.fold_in(_rk, 1), (2, 256, 512), jnp.float32)
        _lenS = 256 - jax.random.randint(jax.random.fold_in(_rk, 7), (2,), 0, max(1, 256 // 4) + 1, jnp.int32)
        _lenS2 = 512 - jax.random.randint(jax.random.fold_in(_rk, 8), (2,), 0, max(1, 512 // 4) + 1, jnp.int32)
        _ctx_4096P = jax.random.normal(jax.random.fold_in(_rk, 11), (2, 16, 512), jnp.float32)
        _ctx_4096c = jax.random.dirichlet(jax.random.fold_in(_rk, 511), 0.3 * jnp.ones((16,), jnp.float32), (2, 512))
        _ctx_4096t = jnp.einsum('bsk,bkd->bsd', _ctx_4096c, _ctx_4096P)
        _ctx_4096t = _ctx_4096t * jax.lax.rsqrt(jnp.mean(jnp.square(_ctx_4096t)) + 1e-12) * 0.953939
        ctx_4096 = -0.000702761 + 1.00443 * (_ctx_4096t + 0.3 * jax.random.normal(jax.random.fold_in(_rk, 611), (2, 512, 512), jnp.float32))
        fside_BxSxS_0 = -0.000132966 + 0.0502041 * jax.random.normal(jax.random.fold_in(_rk, 12), (2, 256, 256), jnp.float32)
        return (x, ctx_4096, fside_BxSxS_0)
    x, ctx_4096, fside_BxSxS_0 = _rec_inputs()

    def _L0_xattn_setup():
        import jax, jax.numpy as jnp
        import numpy as np
        K = 8
        NUM_BLOCKS = 4
        SLOPE = 0.01

        def _lrelu(x):
            return jnp.where(x >= 0, x, SLOPE * x)

        def _knn_indices(xyz, k):
            sq = jnp.sum(xyz * xyz, axis=1)
            d2 = sq[:, :, None] + sq[:, None, :] - 2.0 * jnp.einsum('bdn,bdm->bnm', xyz, xyz)
            _, idx = jax.lax.top_k(-d2, k)
            return idx

        def _group_point(p, idx_t):
            return jnp.take_along_axis(p[:, :, None, :], idx_t, axis=3)
        key = jax.random.key(seed)
        k1, k2, k3, k4 = jax.random.split(key, 4)
        b, n, d = (4, 512, 64)
        xyz = jax.random.normal(k1, (b, 3, n), dtype=jnp.float32)
        points = jax.random.normal(k2, (b, d, n), dtype=jnp.float32)
        w_center = jax.random.normal(k3, (NUM_BLOCKS, d, d), dtype=jnp.float32) * 0.05
        w_neighbor = jax.random.normal(k4, (NUM_BLOCKS, d, d), dtype=jnp.float32) * 0.05
        return {'xyz': xyz, 'points': points, 'w_center': w_center, 'w_neighbor': w_neighbor}
    _L0_xattn_all = _L0_xattn_setup()
    _L0_xattn_in = {k: v for k, v in _L0_xattn_all.items() if k in ()}
    del _L0_xattn_all

    def _L1_xattn_setup():
        import jax, jax.numpy as jnp
        import numpy as np
        K = 8
        NUM_BLOCKS = 4
        SLOPE = 0.01

        def _lrelu(x):
            return jnp.where(x >= 0, x, SLOPE * x)

        def _knn_indices(xyz, k):
            sq = jnp.sum(xyz * xyz, axis=1)
            d2 = sq[:, :, None] + sq[:, None, :] - 2.0 * jnp.einsum('bdn,bdm->bnm', xyz, xyz)
            _, idx = jax.lax.top_k(-d2, k)
            return idx

        def _group_point(p, idx_t):
            return jnp.take_along_axis(p[:, :, None, :], idx_t, axis=3)
        key = jax.random.key(seed)
        k1, k2, k3, k4 = jax.random.split(key, 4)
        b, n, d = (4, 512, 64)
        xyz = jax.random.normal(k1, (b, 3, n), dtype=jnp.float32)
        points = jax.random.normal(k2, (b, d, n), dtype=jnp.float32)
        w_center = jax.random.normal(k3, (NUM_BLOCKS, d, d), dtype=jnp.float32) * 0.05
        w_neighbor = jax.random.normal(k4, (NUM_BLOCKS, d, d), dtype=jnp.float32) * 0.05
        return {'xyz': xyz, 'points': points, 'w_center': w_center, 'w_neighbor': w_neighbor}
    _L1_xattn_all = _L1_xattn_setup()
    _L1_xattn_in = {k: v for k, v in _L1_xattn_all.items() if k in ()}
    del _L1_xattn_all
    return {'x': x, 'ctx_4096': ctx_4096, 'fside_BxSxS_0': fside_BxSxS_0}

def reference(x, ctx_4096, fside_BxSxS_0):
    import jax
    import jax.numpy as jnp

    def _L0_xattn_ref(xyz, points, w_center, w_neighbor):
        import jax, jax.numpy as jnp
        import numpy as np
        K = 8
        NUM_BLOCKS = 4
        SLOPE = 0.01

        def _lrelu(x):
            return jnp.where(x >= 0, x, SLOPE * x)

        def _knn_indices(xyz, k):
            sq = jnp.sum(xyz * xyz, axis=1)
            d2 = sq[:, :, None] + sq[:, None, :] - 2.0 * jnp.einsum('bdn,bdm->bnm', xyz, xyz)
            _, idx = jax.lax.top_k(-d2, k)
            return idx

        def _group_point(p, idx_t):
            return jnp.take_along_axis(p[:, :, None, :], idx_t, axis=3)
        idx = _knn_indices(xyz, K)
        idx_t = jnp.transpose(idx, (0, 2, 1))[:, None, :, :]
        for i in range(NUM_BLOCKS):
            shortcut = points
            p = _lrelu(points)
            g = _group_point(p, idx_t)
            c = jnp.einsum('oi,bin->bon', w_center[i], p)
            gn = jnp.einsum('oi,bikn->bokn', w_neighbor[i], g)
            points = (c + gn.sum(axis=2)) / (K + 1.0) + shortcut
        return points

    def _L1_xattn_ref(xyz, points, w_center, w_neighbor):
        import jax, jax.numpy as jnp
        import numpy as np
        K = 8
        NUM_BLOCKS = 4
        SLOPE = 0.01

        def _lrelu(x):
            return jnp.where(x >= 0, x, SLOPE * x)

        def _knn_indices(xyz, k):
            sq = jnp.sum(xyz * xyz, axis=1)
            d2 = sq[:, :, None] + sq[:, None, :] - 2.0 * jnp.einsum('bdn,bdm->bnm', xyz, xyz)
            _, idx = jax.lax.top_k(-d2, k)
            return idx

        def _group_point(p, idx_t):
            return jnp.take_along_axis(p[:, :, None, :], idx_t, axis=3)
        idx = _knn_indices(xyz, K)
        idx_t = jnp.transpose(idx, (0, 2, 1))[:, None, :, :]
        for i in range(NUM_BLOCKS):
            shortcut = points
            p = _lrelu(points)
            g = _group_point(p, idx_t)
            c = jnp.einsum('oi,bin->bon', w_center[i], p)
            gn = jnp.einsum('oi,bikn->bokn', w_neighbor[i], g)
            points = (c + gn.sum(axis=2)) / (K + 1.0) + shortcut
        return points
    x = _L0_xattn_ref(ctx_4096, x, fside_BxSxS_0, fside_BxSxS_0)
    x = _L1_xattn_ref(ctx_4096, x, fside_BxSxS_0, fside_BxSxS_0)
    return x

_drawn_inputs = setup_inputs


def setup_inputs(seed=0):
    import zlib

    import numpy as np

    out = dict(_drawn_inputs(seed))
    spreads = {}
    factors = {}
    for name, (base, spread) in spreads.items():
        noise = np.random.default_rng([zlib.crc32(name.encode()), seed]).standard_normal(out[name].shape)
        drawn = base * np.exp(spread * noise) if base else spread * noise
        out[name] = jnp.asarray(drawn.astype(out[name].dtype))
    for name, factor in factors.items():
        out[name] = (out[name] * factor).astype(out[name].dtype)
    return out
```

```python
from contextlib import ExitStack

import concourse.bass as bass
from concourse import mybir

P = 128
NEIGHBOURS = 8
NUM_BLOCKS = 4
LAYERS = 2
SLOPE = 0.01
TAKEN = -(2.0 ** 127)

ALU = mybir.AluOpType
ACT = mybir.ActivationFunctionType
F32 = mybir.dt.float32
F32R = mybir.dt.float32r
BF16 = mybir.dt.bfloat16


def graph_blocks_kernel(nc: bass.Bass, x: bass.AP, xyz: bass.AP, w: bass.AP, out: bass.AP):
    B, C, N = x.shape
    D = xyz.shape[1]
    W_COUNT = w.shape[0]
    DT, CT, NT = D // P, C // P, N // P
    STEPS = LAYERS * NUM_BLOCKS
    HALF = NT // 2
    assert B == 2 and W_COUNT == 2 and NT == 4 and CT == 2 and N == 512 and C * HALF == 512

    with ExitStack() as ctx:
        def sb(name, shape, dt):
            return ctx.enter_context(nc.sbuf_tensor(name, shape, dt))

        def sem(name):
            return ctx.enter_context(nc.semaphore(name))

        def sems(name, n):
            return [sem(f"{name}{i}") for i in range(n)]

        xyz_sb = [sb(f"xyz_sb{b}", [P, DT, N], F32) for b in range(B)]
        squares = [sb(f"squares{b}", [P, DT, N], F32) for b in range(B)]
        square_sum = [sb(f"square_sum{b}", [P, DT - 1, N], F32) for b in range(B)]
        norm_col = sb("norm_col", [P, B, NT], F32)
        norm_pair = [sb(f"norm_pair{b}", [P, NT, N], F32) for b in range(B)]
        keys = [sb(f"keys{b}", [P, NT, N], F32) for b in range(B)]
        top8 = sb("top8", [P, B, NT, NEIGHBOURS], F32)
        marked = sb("marked", [P, B, NT, N], BF16)
        mask = [sb(f"mask{b}", [P, NT, N], BF16) for b in range(B)]
        near = [sb(f"near{b}", [P, NT, N], F32R) for b in range(B)]
        w_sb = sb("w_sb", [P, W_COUNT, CT, C], F32)
        wT = sb("wT", [P, W_COUNT, CT, C], F32)
        points = [sb(f"points{b}", [P, CT, N], F32) for b in range(B)]
        p = [sb(f"p{b}", [P, CT, N], F32) for b in range(B)]
        proj_hi = [sb(f"proj_hi{b}", [P, NT, C], F32R) for b in range(B)]
        proj_lo = [sb(f"proj_lo{b}", [P, NT, C], F32R) for b in range(B)]
        ident = sb("ident", [P, P], F32)
        ident_bf = sb("ident_bf", [P, P], BF16)
        ones = sb("ones", [P, P], F32)

        bank = [ctx.enter_context(nc.psum_tensor(f"bank{i}", [P, 512], F32)) for i in range(8)]
        mix_ps = [[bank[0], bank[1]], [bank[2], bank[3]]]
        proj_ps = [[bank[4], bank[5]], [bank[6], bank[7]]]
        gram_ps = [[bank[0], bank[1], bank[2], bank[3]], [bank[4], bank[5], bank[0], bank[1]]]
        norm_row_ps = bank[6]
        norm_col_ps = bank[7]
        keyT_ps = [None, bank[2][:, 0:P], bank[2][:, P:3 * P], bank[3][:, 0:3 * P]]
        wT_ps = [bank[4], bank[5]]
        maskT_ps = [bank[2], bank[3]]

        xyz_loaded = [sems(f"xyz_loaded{b}_", DT) for b in range(B)]
        w_loaded = sem("w_loaded")
        x_loaded = sems("x_loaded", B)
        out_stored = sem("out_stored")
        consts_ready = sem("consts_ready")
        squared = sems("squared", B)
        summed = sems("summed", B)
        norm_col_done = sem("norm_col_done")
        norm_col_copied = sem("norm_col_copied")
        norm_row_done = sem("norm_row_done")
        norm_pair_ready = sems("norm_pair_ready", B)
        gram_done = sems("gram_done", B)
        keys_made = sems("keys_made", B)
        keyT_done = sems("keyT_done", B)
        keyT_copied = sems("keyT_copied", B)
        top8_found = sem("top8_found")
        top8_marked = sem("top8_marked")
        mask_ready = sems("mask_ready", B)
        maskT_done = sems("maskT_done", B)
        near_ready = sems("near_ready", B)
        wT_done = sem("wT_done")
        wT_copied = sem("wT_copied")
        p_ready = sems("p_ready", B)
        projected = sems("projected", B)
        hi_ready = sems("hi_ready", B)
        lo_ready = sems("lo_ready", B)
        mixed = sems("mixed", B)
        updated = sems("updated", B)

        block = ctx.enter_context(nc.Block())

        def rows(r):
            return slice(r * P, (r + 1) * P)

        @block.sync
        def _(sp):
            xyz_tiles = xyz.rearrange("b (t q) n -> b t q n", q=P)
            for t in range(DT):
                sp.dma_start(xyz_sb[0][:, t, :], xyz_tiles[0, t]).then_inc(xyz_loaded[0][t], 16)
            sp.dma_start(points[0][:, :, :], x[0].rearrange("(t q) n -> q t n", q=P)).then_inc(x_loaded[0], 16)
            for t in range(DT):
                sp.dma_start(xyz_sb[1][:, t, :], xyz_tiles[1, t]).then_inc(xyz_loaded[1][t], 16)
            sp.dma_start(points[1][:, :, :], x[1].rearrange("(t q) n -> q t n", q=P)).then_inc(x_loaded[1], 16)
            for s in range(W_COUNT):
                sp.dma_start(w_sb[:, s, :, :], w[s].rearrange("(t q) i -> q t i", q=P)).then_inc(w_loaded, 16)
            for b in range(B):
                for t in range(CT):
                    sp.wait_ge(updated[b], (STEPS - 1) * CT + t + 1)
                    sp.dma_start(out[b, rows(t), :], points[b][:, t, :]).then_inc(out_stored, 16)
            sp.wait_ge(out_stored, 16 * B * CT)

        @block.gpsimd
        def _(pool):
            nc.gpsimd.memset(ones[:, :], 1.0).then_inc(consts_ready, 1)
            nc.gpsimd.memset(ident[:, :], 0.0).then_inc(consts_ready, 1)
            nc.gpsimd.memset(ident_bf[:, :], 0.0).then_inc(consts_ready, 1)
            pool.wait_ge(consts_ready, 3)
            for m in (ident, ident_bf):
                nc.gpsimd.affine_select(out=m[:, :], in_=m[:, :], compare_op=ALU.not_equal, fill=1.0,
                                        base=0, pattern=[[-1, P]], channel_multiplier=1).then_inc(consts_ready, 1)
            for t in range(1, DT):
                pool.wait_ge(squared[1], t + 1)
                if t >= 2:
                    pool.wait_ge(summed[1], t - 1)
                first = squares[1][:, 0, :] if t == 1 else square_sum[1][:, t - 2, :]
                nc.gpsimd.tensor_tensor(square_sum[1][:, t - 1, :], first, squares[1][:, t, :],
                                        ALU.add).then_inc(summed[1], 1)

        @block.scalar
        def _(act):
            def square(b):
                for t in range(DT):
                    act.wait_ge(xyz_loaded[b][t], 16)
                    nc.scalar.activation(squares[b][:, t, :], xyz_sb[b][:, t, :], ACT.Square).then_inc(squared[b], 1)

            def pair_norms(b):
                act.wait_ge(norm_col_done, b + 1)
                nc.scalar.copy(norm_col[:, b, :], norm_col_ps[:, b * NT:(b + 1) * NT]).then_inc(norm_col_copied, 1)
                act.wait_ge(norm_col_copied, b + 1)
                act.wait_ge(norm_row_done, b + 1)
                for r in range(NT):
                    nc.scalar.activation(norm_pair[b][:, r, r * P:N], norm_row_ps[:, r * P:N], ACT.Identity,
                                         bias=norm_col[:, b, r:r + 1]).then_inc(norm_pair_ready[b], 1)

            def copy_keyT(b):
                for r in range(1, NT):
                    act.wait_ge(keyT_done[b], max(r, 2))
                    nc.scalar.copy(keys[b][:, r, 0:r * P], keyT_ps[r]).then_inc(keyT_copied[b], 1)

            def split_hi(b, s):
                for h in range(2):
                    act.wait_ge(projected[b], 2 * s + h + 1)
                    nc.scalar.copy(proj_hi[b][:, h * HALF:(h + 1) * HALF, :],
                                   proj_ps[b][h][:, :].rearrange("q (t c) -> q t c", c=C)).then_inc(hi_ready[b], 1)

            def make_near(b):
                for r in range(NT):
                    act.wait_ge(maskT_done[b], r + 1)
                    nc.scalar.copy(near[b][:, :, rows(r)],
                                   maskT_ps[r % 2][:, :].rearrange("q (t n) -> q t n", n=P)).then_inc(near_ready[b], 1)

            square(0)
            pair_norms(0)
            square(1)
            pair_norms(1)
            copy_keyT(0)
            for s in range(W_COUNT):
                act.wait_ge(wT_done, s + 1)
                nc.scalar.copy(wT[:, s, :, :], wT_ps[s][:, :].rearrange("q (t c) -> q t c", c=C)).then_inc(wT_copied, 1)
            copy_keyT(1)
            split_hi(0, 0)
            make_near(0)
            split_hi(1, 0)
            make_near(1)
            with act.Fori(1, STEPS) as s:
                for b in range(B):
                    split_hi(b, s)

        @block.vector
        def _(dve):
            def leaky(b, t):
                return nc.vector.scalar_tensor_tensor(
                    out=p[b][:, t, :], in0=points[b][:, t, :], scalar=SLOPE, in1=points[b][:, t, :],
                    op0=ALU.mult, op1=ALU.max).then_inc(p_ready[b], 1)

            def first_p(b):
                dve.wait_ge(x_loaded[b], 16)
                for t in range(CT):
                    leaky(b, t)

            def key_row(b, r):
                dve.wait_ge(norm_pair_ready[b], r + 1)
                dve.wait_ge(gram_done[b], r + 1)
                nc.vector.scalar_tensor_tensor(
                    out=keys[b][:, r, r * P:N], in0=gram_ps[b][r][:, 0:N - r * P], scalar=2.0,
                    in1=norm_pair[b][:, r, r * P:N], op0=ALU.mult, op1=ALU.subtract).then_inc(keys_made[b], 1)

            def nearest(b, r):
                k = b * NT + r + 1
                dve.wait_ge(keys_made[b], r + 1)
                if r >= 1:
                    dve.wait_ge(keyT_copied[b], r)
                nc.vector.max(out=top8[:, b, r, :], in_=keys[b][:, r, :]).then_inc(top8_found, 1)
                dve.wait_ge(top8_found, k)
                nc.vector.match_replace(out=marked[:, b, r, :], in_to_replace=top8[:, b, r, :],
                                        in_values=keys[b][:, r, :], imm_value=TAKEN).then_inc(top8_marked, 1)
                dve.wait_ge(top8_marked, k)
                nc.vector.tensor_scalar(out=mask[b][:, r, :], in0=marked[:, b, r, :], scalar1=TAKEN, scalar2=None,
                                        op0=ALU.is_equal).then_inc(mask_ready[b], 1)

            def split_lo(b, s):
                for h in range(2):
                    dve.wait_ge(hi_ready[b], 2 * s + h + 1)
                    tiles = slice(h * HALF, (h + 1) * HALF)
                    nc.vector.tensor_tensor(proj_lo[b][:, tiles, :],
                                            proj_ps[b][h][:, :].rearrange("q (t c) -> q t c", c=C),
                                            proj_hi[b][:, tiles, :].bitcast(F32), ALU.subtract).then_inc(lo_ready[b], 1)

            def update(b, t, s):
                dve.wait_ge(mixed[b], s * CT + t + 1)
                nc.vector.scalar_tensor_tensor(
                    out=points[b][:, t, :], in0=mix_ps[b][t][:, :], scalar=1.0 / (NEIGHBOURS + 1),
                    in1=points[b][:, t, :], op0=ALU.mult, op1=ALU.add).then_inc(updated[b], 1)

            for t in range(1, DT):
                dve.wait_ge(squared[0], t + 1)
                if t >= 2:
                    dve.wait_ge(summed[0], t - 1)
                first = squares[0][:, 0, :] if t == 1 else square_sum[0][:, t - 2, :]
                nc.vector.tensor_tensor(square_sum[0][:, t - 1, :], first, squares[0][:, t, :],
                                        ALU.add).then_inc(summed[0], 1)
            first_p(0)
            for r in range(NT):
                key_row(0, r)
            nearest(0, 0)
            nearest(0, 1)
            key_row(1, 0)
            nearest(0, 2)
            key_row(1, 1)
            nearest(0, 3)
            key_row(1, 2)
            key_row(1, 3)
            first_p(1)
            nearest(1, 0)
            nearest(1, 1)
            split_lo(0, 0)
            nearest(1, 2)
            nearest(1, 3)
            split_lo(1, 0)
            with dve.Fori(1, STEPS) as s:
                for b in range(B):
                    for t in range(CT):
                        update(b, t, s - 1)
                        dve.wait_ge(updated[b], (s - 1) * CT + t + 1)
                        leaky(b, t)
                for b in range(B):
                    split_lo(b, s)
            for b in range(B):
                for t in range(CT):
                    update(b, t, STEPS - 1)

        @block.tensor
        def _(pe):
            def gram(b, r, t):
                return nc.tensor.matmul(gram_ps[b][r][:, 0:N - r * P], xyz_sb[b][:, t, rows(r)],
                                        xyz_sb[b][:, t, r * P:N], start=(t == 0), stop=(t == DT - 1))

            def norms(b):
                total = square_sum[b][:, DT - 2, :]
                pe.wait_ge(summed[b], DT - 1)
                if b >= 1:
                    pe.wait_ge(norm_col_copied, b)
                for r in range(NT):
                    mm = nc.tensor.matmul(norm_col_ps[:, b * NT + r:b * NT + r + 1], total[:, rows(r)],
                                          ones[:, 0:1], start=True, stop=True)
                mm.then_inc(norm_col_done, 1)
                if b >= 1:
                    pe.wait_ge(norm_pair_ready[b - 1], NT)
                nc.tensor.matmul(norm_row_ps[:, :], ones[:, :], total, start=True, stop=True).then_inc(norm_row_done, 1)

            def transpose_keys(b, r):
                pe.wait_ge(keys_made[b], r + 1)
                for j in range(r + 1, NT):
                    mm = nc.tensor.transpose(keyT_ps[j][:, rows(r)], keys[b][:, r, rows(j)], ident[:, :])
                mm.then_inc(keyT_done[b], 1)

            def transpose_mask(b, r):
                pe.wait_ge(mask_ready[b], r + 1)
                if r >= 2:
                    pe.wait_ge(near_ready[b], r - 1)
                elif b == 0:
                    pe.wait_ge(keyT_copied[1], NT - 1)
                else:
                    pe.wait_ge(near_ready[b - 1], NT - 1 + r)
                for j in range(NT):
                    mm = nc.tensor.matmul(maskT_ps[r % 2][:, rows(j)], mask[b][:, r, rows(j)], ident_bf[:, :],
                                          start=True, stop=(j != r))
                    if j == r:
                        mm = nc.tensor.matmul(maskT_ps[r % 2][:, rows(j)], ident_bf[:, :], ident_bf[:, :],
                                              start=False, stop=True)
                mm.then_inc(maskT_done[b], 1)

            def project(b, s, weight):
                pe.wait_ge(p_ready[b], s * CT + CT)
                for m in range(NT):
                    to = proj_ps[b][m // HALF][:, (m % HALF) * C:(m % HALF + 1) * C]
                    for t in range(CT):
                        mm = nc.tensor.matmul(to, p[b][:, t, rows(m)], weight(t), start=(t == 0), stop=(t == CT - 1))
                    if m % HALF == HALF - 1:
                        mm.then_inc(projected[b], 1)

            def mix(b, s):
                pe.wait_ge(hi_ready[b], 2 * s + 2)
                for o in range(CT):
                    for part in (proj_hi[b], proj_lo[b]):
                        if part is proj_lo[b] and o == 0:
                            pe.wait_ge(lo_ready[b], 2 * s + 2)
                        for m in range(NT):
                            mm = nc.tensor.matmul(mix_ps[b][o][:, :], part[:, m, rows(o)], near[b][:, m, :],
                                                  start=(part is proj_hi[b] and m == 0),
                                                  stop=(part is proj_lo[b] and m == NT - 1))
                    mm.then_inc(mixed[b], 1)

            for t in range(DT):
                pe.wait_ge(xyz_loaded[0][t], 16)
                if t == DT - 1:
                    pe.wait_ge(consts_ready, 5)
                    norms(0)
                for r in range(NT):
                    mm = gram(0, r, t)
                    if t == DT - 1:
                        mm.then_inc(gram_done[0], 1)
            for t in range(DT):
                pe.wait_ge(xyz_loaded[1][t], 16)
            for r in range(NT):
                if r >= 2:
                    pe.wait_ge(keys_made[0], r - 1)
                for t in range(DT):
                    mm = gram(1, r, t)
                mm.then_inc(gram_done[1], 1)
                if r == 0:
                    norms(1)
                    pe.wait_ge(keys_made[0], NT)
                    for i in range(NT - 1):
                        transpose_keys(0, i)
            pe.wait_ge(w_loaded, 16 * W_COUNT)
            for s in range(W_COUNT):
                pe.wait_ge(keys_made[1], s + 1)
                for i in range(CT):
                    for o in range(CT):
                        mm = nc.tensor.transpose(wT_ps[s][:, i * C + o * P:i * C + (o + 1) * P],
                                                 w_sb[:, s, o, rows(i)], ident[:, :])
                mm.then_inc(wT_done, 1)
            pe.wait_ge(keyT_copied[0], NT - 1)
            for r in range(NT - 1):
                transpose_keys(1, r)
            pe.wait_ge(wT_copied, W_COUNT)
            project(0, 0, lambda t: wT[:, 0, t, :])
            for r in range(NT):
                transpose_mask(0, r)
            pe.wait_ge(norm_pair_ready[1], NT)
            project(1, 0, lambda t: wT[:, 0, t, :])
            pe.wait_ge(near_ready[0], NT)
            pe.wait_ge(keys_made[1], NT)
            mix(0, 0)
            for r in range(NT):
                transpose_mask(1, r)
            pe.wait_ge(near_ready[1], NT)
            mix(1, 0)
            with pe.Fori(1, STEPS) as s:
                slot = (((s & (NUM_BLOCKS - 1)) + (NUM_BLOCKS - 1)) >> 2) & 1
                for b in range(B):
                    project(b, s, lambda t: wT[:, slot, t, :])
                for b in range(B):
                    mix(b, s)


_INS = ['x', 'ctx_4096', 'fside_BxSxS_0']


def kernel(**inputs):
    import numpy as _np
    import concourse.bacc as _bacc
    from concourse import mybir as _mybir
    from concourse.bass_utils import run_bass_kernel_spmd as _run

    nc = _bacc.Bacc("TRN2", target_bir_lowering=False, num_devices=1)
    arrays, args = {}, []
    for name in _INS:
        a = _np.ascontiguousarray(inputs[name])
        arrays[f"in_{name}_dram"] = a
        args.append(nc.dram_tensor(f"in_{name}_dram", a.shape, _mybir.dt.from_np(a.dtype), kind="ExternalInput").ap())
    out = nc.dram_tensor("out_0_dram", inputs['x'].shape, _mybir.dt.float32, kind="ExternalOutput").ap()
    graph_blocks_kernel(nc, *args, out)
    r = _run(nc, [arrays], core_ids=[0])
    return r.results[0]["out_0_dram"]
```

```python
from contextlib import ExitStack

import concourse.bass as bass
from concourse import mybir

P = 128
NEIGHBOURS = 8
NUM_BLOCKS = 4
LAYERS = 2
SLOPE = 0.01
TAKEN = -(2.0 ** 127)
WARM_UP = 5

ALU = mybir.AluOpType
ACT = mybir.ActivationFunctionType
F32 = mybir.dt.float32
F32R = mybir.dt.float32r
BF16 = mybir.dt.bfloat16


def graph_blocks_kernel(nc: bass.Bass, x: bass.AP, xyz: bass.AP, w: bass.AP, out: bass.AP):
    B, C, N = x.shape
    D = xyz.shape[1]
    W_COUNT = w.shape[0]
    DT, CT, NT = D // P, C // P, N // P
    STEPS = LAYERS * NUM_BLOCKS
    HALF = NT // 2
    assert B == 2 and W_COUNT == 2 and NT == 4 and CT == 2 and N == 512 and C * HALF == 512

    with ExitStack() as ctx:
        def sb(name, shape, dt):
            return ctx.enter_context(nc.sbuf_tensor(name, shape, dt))

        def sem(name):
            return ctx.enter_context(nc.semaphore(name))

        def sems(name, n):
            return [sem(f"{name}{i}") for i in range(n)]

        xyz_sb = [sb(f"xyz_sb{b}", [P, DT, N], F32) for b in range(B)]
        squares = [sb(f"squares{b}", [P, DT, N], F32) for b in range(B)]
        square_sum = [sb(f"square_sum{b}", [P, DT - 1, N], F32) for b in range(B)]
        square_sum_hi = [sb(f"square_sum_hi{b}", [P, N], F32R) for b in range(B)]
        square_sum_lo = [sb(f"square_sum_lo{b}", [P, N], F32R) for b in range(B)]
        norm_col = sb("norm_col", [P, B, NT], F32)
        norm_pair = [sb(f"norm_pair{b}", [P, NT, N], F32) for b in range(B)]
        keys = [sb(f"keys{b}", [P, NT, N], F32) for b in range(B)]
        top8 = sb("top8", [P, B, NT, NEIGHBOURS], F32)
        marked = sb("marked", [P, B, NT, N], BF16)
        mask = [sb(f"mask{b}", [P, NT, N], BF16) for b in range(B)]
        near = [sb(f"near{b}", [P, NT, N], F32R) for b in range(B)]
        w_sb = sb("w_sb", [P, W_COUNT, CT, C], F32)
        wT = sb("wT", [P, W_COUNT, CT, C], F32)
        points = [sb(f"points{b}", [P, CT, N], F32) for b in range(B)]
        p = [sb(f"p{b}", [P, CT, N], F32) for b in range(B)]
        proj_hi = [sb(f"proj_hi{b}", [P, NT, C], F32R) for b in range(B)]
        proj_lo = [sb(f"proj_lo{b}", [P, NT, C], F32R) for b in range(B)]
        ident = sb("ident", [P, P], F32)
        ident_bf = sb("ident_bf", [P, P], BF16)
        ones = sb("ones", [P, P], F32R)
        zeros = sb("zeros", [P, N], BF16)

        bank = [ctx.enter_context(nc.psum_tensor(f"bank{i}", [P, 512], F32)) for i in range(8)]
        mix_ps = [[bank[0], bank[1]], [bank[2], bank[3]]]
        proj_ps = [[bank[4], bank[5]], [bank[6], bank[7]]]
        gram_ps = [[bank[0], bank[1], bank[2], bank[3]], [bank[4], bank[5], bank[0], bank[1]]]
        norm_row_ps = bank[6]
        norm_col_ps = bank[7]
        keyT_ps = [None, bank[2][:, 0:P], bank[2][:, P:3 * P], bank[3][:, 0:3 * P]]
        wT_ps = [bank[6], bank[7]]
        maskT_ps = [[bank[0], bank[1], bank[2], bank[3]], [bank[2], bank[3], bank[4], bank[5]]]
        warm_ps = bank[7]

        xyz_loaded = [sems(f"xyz_loaded{b}_", DT) for b in range(B)]
        w_loaded = sem("w_loaded")
        x_loaded = sems("x_loaded", B)
        out_stored = sem("out_stored")
        zeros_ready = sem("zeros_ready")
        consts_ready = sem("consts_ready")
        squared = sems("squared", B)
        summed = sems("summed", B)
        sum_hi_ready = sems("sum_hi_ready", B)
        sum_lo_ready = sems("sum_lo_ready", B)
        norm_col_done = sem("norm_col_done")
        norm_col_copied = sem("norm_col_copied")
        norm_row_done = sem("norm_row_done")
        norm_pair_ready = sems("norm_pair_ready", B)
        gram_done = sems("gram_done", B)
        keys_made = sems("keys_made", B)
        keyT_done = sems("keyT_done", B)
        keyT_copied = sems("keyT_copied", B)
        top8_found = sem("top8_found")
        top8_marked = sem("top8_marked")
        mask_ready = sems("mask_ready", B)
        maskT_done = sems("maskT_done", B)
        near_ready = sems("near_ready", B)
        wT_done = sem("wT_done")
        wT_copied = sem("wT_copied")
        p_ready = sems("p_ready", B)
        projected = sems("projected", B)
        hi_ready = sems("hi_ready", B)
        lo_ready = sems("lo_ready", B)
        mixed = sems("mixed", B)
        updated = sems("updated", B)

        block = ctx.enter_context(nc.Block())

        def rows(r):
            return slice(r * P, (r + 1) * P)

        @block.sync
        def _(sp):
            xyz_tiles = xyz.rearrange("b (t q) n -> b t q n", q=P)
            for t in range(DT):
                sp.dma_start(xyz_sb[0][:, t, :], xyz_tiles[0, t]).then_inc(xyz_loaded[0][t], 16)
            for t in range(DT):
                sp.dma_start(xyz_sb[1][:, t, :], xyz_tiles[1, t]).then_inc(xyz_loaded[1][t], 16)
            for b in range(B):
                sp.dma_start(points[b][:, :, :], x[b].rearrange("(t q) n -> q t n", q=P)).then_inc(x_loaded[b], 16)
            for s in range(W_COUNT):
                sp.dma_start(w_sb[:, s, :, :], w[s].rearrange("(t q) i -> q t i", q=P)).then_inc(w_loaded, 16)
            for b in range(B):
                for t in range(CT):
                    sp.wait_ge(updated[b], (STEPS - 1) * CT + t + 1)
                    sp.dma_start(out[b, rows(t), :], points[b][:, t, :]).then_inc(out_stored, 16)
            sp.wait_ge(out_stored, 16 * B * CT)

        @block.gpsimd
        def _(pool):
            nc.gpsimd.memset(ones[:, :].bitcast(F32), 1.0).then_inc(consts_ready, 1)
            nc.gpsimd.memset(ident[:, :], 0.0).then_inc(consts_ready, 1)
            nc.gpsimd.memset(ident_bf[:, :], 0.0).then_inc(consts_ready, 1)
            pool.wait_ge(consts_ready, 3)
            for m in (ident, ident_bf):
                nc.gpsimd.affine_select(out=m[:, :], in_=m[:, :], compare_op=ALU.not_equal, fill=1.0,
                                        base=0, pattern=[[-1, P]], channel_multiplier=1).then_inc(consts_ready, 1)

        @block.scalar
        def _(act):
            def square(b):
                for t in range(DT):
                    act.wait_ge(xyz_loaded[b][t], 16)
                    nc.scalar.activation(squares[b][:, t, :], xyz_sb[b][:, t, :], ACT.Square).then_inc(squared[b], 1)

            def sum_hi(b):
                act.wait_ge(summed[b], DT - 1)
                nc.scalar.copy(square_sum_hi[b][:, :], square_sum[b][:, DT - 2, :]).then_inc(sum_hi_ready[b], 1)

            def pair_norms(b):
                act.wait_ge(norm_col_done, b + 1)
                nc.scalar.copy(norm_col[:, b, :], norm_col_ps[:, b * 2 * NT:(b + 1) * 2 * NT:2]).then_inc(norm_col_copied, 1)
                act.wait_ge(norm_col_copied, b + 1)
                act.wait_ge(norm_row_done, b + 1)
                for r in range(NT):
                    nc.scalar.activation(norm_pair[b][:, r, r * P:N], norm_row_ps[:, r * P:N], ACT.Identity,
                                         bias=norm_col[:, b, r:r + 1]).then_inc(norm_pair_ready[b], 1)

            def copy_keyT(b):
                for r in range(1, NT):
                    act.wait_ge(keyT_done[b], max(r, 2))
                    nc.scalar.copy(keys[b][:, r, 0:r * P], keyT_ps[r]).then_inc(keyT_copied[b], 1)

            def split_hi(b, s):
                for h in range(2):
                    act.wait_ge(projected[b], 2 * s + h + 1)
                    nc.scalar.copy(proj_hi[b][:, h * HALF:(h + 1) * HALF, :],
                                   proj_ps[b][h][:, :].rearrange("q (t c) -> q t c", c=C)).then_inc(hi_ready[b], 1)

            def make_near(b):
                for r in range(NT):
                    act.wait_ge(maskT_done[b], r + 1)
                    nc.scalar.copy(near[b][:, :, rows(r)],
                                   maskT_ps[b][r][:, :].rearrange("q (t n) -> q t n", n=P)).then_inc(near_ready[b], 1)

            square(0)
            sum_hi(0)
            square(1)
            pair_norms(0)
            sum_hi(1)
            copy_keyT(0)
            pair_norms(1)
            for s in range(W_COUNT):
                act.wait_ge(wT_done, s + 1)
                nc.scalar.copy(wT[:, s, :, :], wT_ps[s][:, :].rearrange("q (t c) -> q t c", c=C)).then_inc(wT_copied, 1)
            copy_keyT(1)
            split_hi(0, 0)
            make_near(0)
            split_hi(1, 0)
            make_near(1)
            with act.Fori(1, STEPS) as s:
                for b in range(B):
                    split_hi(b, s)

        @block.vector
        def _(dve):
            def sum_squares(b):
                for t in range(1, DT):
                    dve.wait_ge(squared[b], t + 1)
                    if t >= 2:
                        dve.wait_ge(summed[b], t - 1)
                    first = squares[b][:, 0, :] if t == 1 else square_sum[b][:, t - 2, :]
                    nc.vector.tensor_tensor(square_sum[b][:, t - 1, :], first, squares[b][:, t, :],
                                            ALU.add).then_inc(summed[b], 1)
                dve.wait_ge(sum_hi_ready[b], 1)
                nc.vector.tensor_tensor(square_sum_lo[b][:, :], square_sum[b][:, DT - 2, :],
                                        square_sum_hi[b][:, :].bitcast(F32), ALU.subtract).then_inc(sum_lo_ready[b], 1)

            def leaky(b, t):
                return nc.vector.scalar_tensor_tensor(
                    out=p[b][:, t, :], in0=points[b][:, t, :], scalar=SLOPE, in1=points[b][:, t, :],
                    op0=ALU.mult, op1=ALU.max).then_inc(p_ready[b], 1)

            def first_p(b):
                dve.wait_ge(x_loaded[b], 16)
                for t in range(CT):
                    leaky(b, t)

            def key_row(b, r):
                dve.wait_ge(norm_pair_ready[b], r + 1)
                dve.wait_ge(gram_done[b], r + 1)
                nc.vector.scalar_tensor_tensor(
                    out=keys[b][:, r, r * P:N], in0=gram_ps[b][r][:, 0:N - r * P], scalar=2.0,
                    in1=norm_pair[b][:, r, r * P:N], op0=ALU.mult, op1=ALU.subtract).then_inc(keys_made[b], 1)

            def nearest(b, r):
                k = b * NT + r + 1
                dve.wait_ge(keys_made[b], r + 1)
                if r >= 1:
                    dve.wait_ge(keyT_copied[b], r)
                nc.vector.max(out=top8[:, b, r, :], in_=keys[b][:, r, :]).then_inc(top8_found, 1)
                dve.wait_ge(top8_found, k)
                nc.vector.match_replace(out=marked[:, b, r, :], in_to_replace=top8[:, b, r, :],
                                        in_values=keys[b][:, r, :], imm_value=TAKEN).then_inc(top8_marked, 1)
                dve.wait_ge(top8_marked, k)
                nc.vector.tensor_scalar(out=mask[b][:, r, :], in0=marked[:, b, r, :], scalar1=TAKEN, scalar2=None,
                                        op0=ALU.is_equal).then_inc(mask_ready[b], 1)

            def split_lo(b, s):
                for h in range(2):
                    dve.wait_ge(hi_ready[b], 2 * s + h + 1)
                    tiles = slice(h * HALF, (h + 1) * HALF)
                    nc.vector.tensor_tensor(proj_lo[b][:, tiles, :],
                                            proj_ps[b][h][:, :].rearrange("q (t c) -> q t c", c=C),
                                            proj_hi[b][:, tiles, :].bitcast(F32), ALU.subtract).then_inc(lo_ready[b], 1)

            def update(b, t, s):
                dve.wait_ge(mixed[b], s * CT + t + 1)
                nc.vector.scalar_tensor_tensor(
                    out=points[b][:, t, :], in0=mix_ps[b][t][:, :], scalar=1.0 / (NEIGHBOURS + 1),
                    in1=points[b][:, t, :], op0=ALU.mult, op1=ALU.add).then_inc(updated[b], 1)

            nc.vector.memset(zeros[:, :], 0.0).then_inc(zeros_ready, 1)
            sum_squares(0)
            sum_squares(1)
            first_p(0)
            for r in range(NT):
                key_row(0, r)
            nearest(0, 0)
            first_p(1)
            nearest(0, 1)
            key_row(1, 0)
            nearest(0, 2)
            for r in range(1, NT):
                key_row(1, r)
            nearest(0, 3)
            nearest(1, 0)
            nearest(1, 1)
            split_lo(0, 0)
            nearest(1, 2)
            nearest(1, 3)
            split_lo(1, 0)
            with dve.Fori(1, STEPS) as s:
                for b in range(B):
                    for t in range(CT):
                        update(b, t, s - 1)
                        dve.wait_ge(updated[b], (s - 1) * CT + t + 1)
                        leaky(b, t)
                for b in range(B):
                    split_lo(b, s)
            for b in range(B):
                for t in range(CT):
                    update(b, t, STEPS - 1)

        @block.tensor
        def _(pe):
            def gram(b, r, t):
                return nc.tensor.matmul(gram_ps[b][r][:, 0:N - r * P], xyz_sb[b][:, t, rows(r)],
                                        xyz_sb[b][:, t, r * P:N], start=(t == 0), stop=(t == DT - 1))

            def norms(b):
                parts = (square_sum_hi[b], square_sum_lo[b])
                pe.wait_ge(sum_lo_ready[b], 1)
                if b >= 1:
                    pe.wait_ge(norm_col_copied, b)
                for r in range(NT):
                    to = norm_col_ps[:, (b * NT + r) * 2:(b * NT + r + 1) * 2]
                    for i, part in enumerate(parts):
                        mm = nc.tensor.matmul(to, part[:, rows(r)], ones[:, 0:2], start=(i == 0), stop=(i == 1))
                mm.then_inc(norm_col_done, 1)
                if b >= 1:
                    pe.wait_ge(norm_pair_ready[b - 1], NT)
                for i, part in enumerate(parts):
                    mm = nc.tensor.matmul(norm_row_ps[:, :], ones[:, :], part[:, :], start=(i == 0), stop=(i == 1))
                mm.then_inc(norm_row_done, 1)

            def transpose_keys(b, r):
                pe.wait_ge(keys_made[b], r + 1)
                for j in range(r + 1, NT):
                    mm = nc.tensor.transpose(keyT_ps[j][:, rows(r)], keys[b][:, r, rows(j)], ident[:, :])
                mm.then_inc(keyT_done[b], 1)

            def transpose_mask(b, r):
                pe.wait_ge(mask_ready[b], r + 1)
                for j in range(NT):
                    mm = nc.tensor.matmul(maskT_ps[b][r][:, rows(j)], mask[b][:, r, rows(j)], ident_bf[:, :],
                                          start=True, stop=(j != r))
                    if j == r:
                        mm = nc.tensor.matmul(maskT_ps[b][r][:, rows(j)], ident_bf[:, :], ident_bf[:, :],
                                              start=False, stop=True)
                mm.then_inc(maskT_done[b], 1)

            def project(b, s, weight):
                pe.wait_ge(p_ready[b], s * CT + CT)
                for m in range(NT):
                    to = proj_ps[b][m // HALF][:, (m % HALF) * C:(m % HALF + 1) * C]
                    for t in range(CT):
                        mm = nc.tensor.matmul(to, p[b][:, t, rows(m)], weight(t), start=(t == 0), stop=(t == CT - 1))
                    if m % HALF == HALF - 1:
                        mm.then_inc(projected[b], 1)

            def mix_tile(b, s, o):
                if o == 0:
                    pe.wait_ge(hi_ready[b], 2 * s + 2)
                for part in (proj_hi[b], proj_lo[b]):
                    if part is proj_lo[b] and o == 0:
                        pe.wait_ge(lo_ready[b], 2 * s + 2)
                    for m in range(NT):
                        mm = nc.tensor.matmul(mix_ps[b][o][:, :], part[:, m, rows(o)], near[b][:, m, :],
                                              start=(part is proj_hi[b] and m == 0),
                                              stop=(part is proj_lo[b] and m == NT - 1))
                mm.then_inc(mixed[b], 1)

            pe.wait_ge(zeros_ready, 1)
            for _ in range(WARM_UP):
                nc.tensor.matmul(warm_ps[:, :], zeros[:, 0:P], zeros[:, :], start=True, stop=True)

            for t in range(DT):
                pe.wait_ge(xyz_loaded[0][t], 16)
                if t == DT // 2:
                    pe.wait_ge(consts_ready, 5)
                    norms(0)
                for r in range(NT):
                    mm = gram(0, r, t)
                    if t == DT - 1:
                        mm.then_inc(gram_done[0], 1)

            for r in range(NT):
                if r >= 2:
                    pe.wait_ge(keys_made[0], r - 1)
                for t in range(DT):
                    if r == 0:
                        pe.wait_ge(xyz_loaded[1][t], 16)
                    mm = gram(1, r, t)
                    if r == 0 and t == DT // 2:
                        pe.wait_ge(keys_made[0], NT)
                        for i in range(NT - 1):
                            transpose_keys(0, i)
                mm.then_inc(gram_done[1], 1)
                if r == 0:
                    norms(1)

            pe.wait_ge(w_loaded, 16 * W_COUNT)
            pe.wait_ge(norm_pair_ready[1], NT)
            for s in range(W_COUNT):
                for i in range(CT):
                    for o in range(CT):
                        mm = nc.tensor.transpose(wT_ps[s][:, i * C + o * P:i * C + (o + 1) * P],
                                                 w_sb[:, s, o, rows(i)], ident[:, :])
                mm.then_inc(wT_done, 1)
            pe.wait_ge(keyT_copied[0], NT - 1)
            for r in range(NT - 1):
                transpose_keys(1, r)

            pe.wait_ge(keys_made[1], NT)
            pe.wait_ge(wT_copied, W_COUNT)
            project(0, 0, lambda t: wT[:, 0, t, :])
            pe.wait_ge(keyT_copied[1], NT - 1)
            for r in range(NT):
                transpose_mask(0, r)
            project(1, 0, lambda t: wT[:, 0, t, :])
            pe.wait_ge(near_ready[0], NT)
            pe.wait_ge(lo_ready[0], 2)
            for r in range(NT // 2):
                transpose_mask(1, r)
            mix_tile(0, 0, 0)
            for r in range(NT // 2, NT):
                transpose_mask(1, r)
            mix_tile(0, 0, 1)
            pe.wait_ge(near_ready[1], NT)
            for o in range(CT):
                mix_tile(1, 0, o)
            with pe.Fori(1, STEPS) as s:
                slot = (((s & (NUM_BLOCKS - 1)) + (NUM_BLOCKS - 1)) >> 2) & 1
                for b in range(B):
                    project(b, s, lambda t: wT[:, slot, t, :])
                for b in range(B):
                    for o in range(CT):
                        mix_tile(b, s, o)


_INS = ['x', 'ctx_4096', 'fside_BxSxS_0']


def kernel(**inputs):
    import numpy as _np
    import concourse.bacc as _bacc
    from concourse import mybir as _mybir
    from concourse.bass_utils import run_bass_kernel_spmd as _run

    nc = _bacc.Bacc("TRN2", target_bir_lowering=False, num_devices=1)
    arrays, args = {}, []
    for name in _INS:
        a = _np.ascontiguousarray(inputs[name])
        arrays[f"in_{name}_dram"] = a
        args.append(nc.dram_tensor(f"in_{name}_dram", a.shape, _mybir.dt.from_np(a.dtype), kind="ExternalInput").ap())
    out = nc.dram_tensor("out_0_dram", inputs['x'].shape, _mybir.dt.float32, kind="ExternalOutput").ap()
    graph_blocks_kernel(nc, *args, out)
    r = _run(nc, [arrays], core_ids=[0])
    return r.results[0]["out_0_dram"]
```
